# Optimizing a Trainium2 kernel written in Bass

```python
import numpy as np
import jax
import jax.numpy as jnp

def _softmax(x, axis=-1):
    return jax.nn.softmax(x, axis=axis)

def _gelu(x):
    return jax.nn.gelu(x, approximate=True)

def _silu(x):
    return jax.nn.silu(x)

def _sigmoid(x):
    return jax.nn.sigmoid(x)

def _layernorm(x, axis=-1, eps=1e-05):
    m = jnp.mean(x, axis=axis, keepdims=True)
    v = jnp.var(x, axis=axis, keepdims=True)
    return (x - m) / jnp.sqrt(v + eps)

def _scatter_add(tgt, idx, src, axis=0):
    return tgt.at[idx].add(src)

def _segment_sum(src, seg, n):
    return jax.ops.segment_sum(src, seg, n)
kernel_name = 'mk_flamingo_gated_d1_seqx_r4_1924ad'

def setup_inputs(seed: int=0):
    np.random.seed(seed)
    _w = jnp.asarray

    def _rec_inputs():
        import jax
        import jax.numpy as jnp
        _rk = jax.random.key(seed)
        x = 7.22e-05 + 1 * jax.random.normal(jax.random.fold_in(_rk, 1), (32, 128, 256), jnp.float32)
        _lenS = 128 - jax.random.randint(jax.random.fold_in(_rk, 7), (32,), 0, max(1, 128 // 4) + 1, jnp.int32)
        _lenS2 = 128 - jax.random.randint(jax.random.fold_in(_rk, 8), (32,), 0, max(1, 128 // 4) + 1, jnp.int32)
        _ctx_1024P = jax.random.normal(jax.random.fold_in(_rk, 11), (32, 16, 256), jnp.float32)
        _ctx_1024c = jax.random.dirichlet(jax.random.fold_in(_rk, 511), 0.3 * jnp.ones((16,), jnp.float32), (32, 128))
        _ctx_1024t = jnp.einsum('bsk,bkd->bsd', _ctx_1024c, _ctx_1024P)
        _ctx_1024t = _ctx_1024t * jax.lax.rsqrt(jnp.mean(jnp.square(_ctx_1024t)) + 1e-12) * 0.953939
        ctx_1024 = 4.13588e-05 + 0.999923 * (_ctx_1024t + 0.3 * jax.random.normal(jax.random.fold_in(_rk, 611), (32, 128, 256), jnp.float32))
        _g = jax.random.normal(jax.random.fold_in(_rk, 9001), (2, 1), jnp.float32)
        _g = jnp.sign(_g) * jnp.maximum(jnp.abs(_g), 1.0) + (_g == 0) * 1.0
        g_xattn = _g[0]
        g_ffn = _g[1]
        return (x, ctx_1024, g_xattn, g_ffn)
    x, ctx_1024, g_xattn, g_ffn = _rec_inputs()

    def _L0_xattn_setup():
        import jax, jax.numpy as jnp
        import numpy as np
        from jax import lax
        NUM_HEADS = 16
        DIM = 256
        BATCH = 4
        SEQ = 512
        key = jax.random.key(seed)
        ks = jax.random.split(key, 12)
        f32 = jnp.float32
        q = jax.random.normal(ks[0], (BATCH, SEQ, DIM), dtype=f32)
        k = jax.random.normal(ks[1], (BATCH, SEQ, DIM), dtype=f32)
        v = jax.random.normal(ks[2], (BATCH, SEQ, DIM), dtype=f32)
        lim = 1.0 / np.sqrt(DIM)
        Wi = jax.random.uniform(ks[3], (DIM, DIM), minval=-lim, maxval=lim, dtype=f32)
        bi = jax.random.uniform(ks[4], (DIM,), minval=-lim, maxval=lim, dtype=f32)
        Wg = jax.random.uniform(ks[5], (DIM, DIM), minval=-lim, maxval=lim, dtype=f32)
        bg = jax.random.uniform(ks[6], (DIM,), minval=-lim, maxval=lim, dtype=f32)
        Wo = jax.random.uniform(ks[7], (DIM, DIM), minval=-lim, maxval=lim, dtype=f32)
        bo = jax.random.uniform(ks[8], (DIM,), minval=-lim, maxval=lim, dtype=f32)
        A = jax.random.normal(ks[9], (DIM, DIM), dtype=f32) * 0.1
        Bm = jax.random.normal(ks[10], (DIM, DIM), dtype=f32) * 0.1
        decay = jnp.full((1, NUM_HEADS, 1), 0.9, dtype=f32)
        return dict(q=q, k=k, v=v, Wi=Wi, bi=bi, Wg=Wg, bg=bg, A=A, Bm=Bm, Wo=Wo, bo=bo, decay=decay)
    _L0_xattn_all = _L0_xattn_setup()
    _L0_xattn_in = {k: v for k, v in _L0_xattn_all.items() if k in ('Wi', 'bi', 'Wg', 'bg', 'A', 'Bm', 'Wo', 'bo', 'decay')}
    del _L0_xattn_all

    def _L0_ffn_setup():
        import jax, jax.numpy as jnp
        import numpy as np
        EPS = 1e-05

        def _quantize(W):
            gamma = jnp.mean(jnp.abs(W))
            return jnp.clip(jnp.round(W / (gamma + EPS)), -1.0, 1.0)
        key = jax.random.key(seed)
        k_x, k_w1, k_b1, k_w2, k_b2 = jax.random.split(key, 5)
        n_embd = 256
        d_ff = 4 * n_embd
        B, S = (4, 1024)
        bound1 = 1.0 / np.sqrt(n_embd)
        bound2 = 1.0 / np.sqrt(d_ff)
        x = jax.random.normal(k_x, (B, S, n_embd), dtype=jnp.float32)
        W1 = jax.random.uniform(k_w1, (d_ff, n_embd), jnp.float32, -bound1, bound1)
        b1 = jax.random.uniform(k_b1, (d_ff,), jnp.float32, -bound1, bound1)
        W2 = jax.random.uniform(k_w2, (n_embd, d_ff), jnp.float32, -bound2, bound2)
        b2 = jax.random.uniform(k_b2, (n_embd,), jnp.float32, -bound2, bound2)
        return {'x': x, 'W1': W1, 'b1': b1, 'W2': W2, 'b2': b2}
    _L0_ffn_all = _L0_ffn_setup()
    _L0_ffn_in = {k: v for k, v in _L0_ffn_all.items() if k in ('W1', 'b1', 'W2', 'b2')}
    del _L0_ffn_all
    return {'x': x, 'ctx_1024': ctx_1024, 'g_xattn': g_xattn, 'g_ffn': g_ffn, 'L0_xattn_Wi': _L0_xattn_in['Wi'], 'L0_xattn_bi': _L0_xattn_in['bi'], 'L0_xattn_Wg': _L0_xattn_in['Wg'], 'L0_xattn_bg': _L0_xattn_in['bg'], 'L0_xattn_A': _L0_xattn_in['A'], 'L0_xattn_Bm': _L0_xattn_in['Bm'], 'L0_xattn_Wo': _L0_xattn_in['Wo'], 'L0_xattn_bo': _L0_xattn_in['bo'], 'L0_xattn_decay': _L0_xattn_in['decay'], 'L0_ffn_W1': _L0_ffn_in['W1'], 'L0_ffn_b1': _L0_ffn_in['b1'], 'L0_ffn_W2': _L0_ffn_in['W2'], 'L0_ffn_b2': _L0_ffn_in['b2']}

def reference(x, ctx_1024, g_xattn, g_ffn, L0_xattn_Wi, L0_xattn_bi, L0_xattn_Wg, L0_xattn_bg, L0_xattn_A, L0_xattn_Bm, L0_xattn_Wo, L0_xattn_bo, L0_xattn_decay, L0_ffn_W1, L0_ffn_b1, L0_ffn_W2, L0_ffn_b2):
    import jax
    import jax.numpy as jnp

    def _L0_xattn_ref(q, k, v, Wi, bi, Wg, bg, A, Bm, Wo, bo, decay):
        import jax, jax.numpy as jnp
        import numpy as np
        from jax import lax
        NUM_HEADS = 16
        DIM = 256
        BATCH = 4
        SEQ = 512
        B, S, D = q.shape
        H = decay.shape[1]
        hd = D // H
        qh = jnp.moveaxis(q.reshape(B, S, H, hd), 1, 0)
        kh = jnp.moveaxis(k.reshape(B, S, H, hd), 1, 0)
        vh = jnp.moveaxis(v.reshape(B, S, H, hd), 1, 0)

        def step(carry, xs):
            r, state = carry
            qt, kt, vt = xs
            r = decay * r + kt * vt
            retained = (qt * r).reshape(B, D)
            inp = retained @ Wi.T + bi
            gate = jax.nn.sigmoid(inp @ Wg.T + bg)
            blended = gate * state + (1.0 - gate) * inp
            state = jnp.tanh(blended @ A.T + inp @ Bm.T)
            out = state @ Wo.T + bo
            return ((r, state), out)
        r0 = jnp.zeros((B, H, hd), dtype=q.dtype)
        s0 = jnp.zeros((B, D), dtype=q.dtype)
        _, outs = lax.scan(step, (r0, s0), (qh, kh, vh))
        return jnp.moveaxis(outs, 0, 1)

    def _L0_ffn_ref(x, W1, b1, W2, b2):
        import jax, jax.numpy as jnp
        import numpy as np
        EPS = 1e-05

        def _quantize(W):
            gamma = jnp.mean(jnp.abs(W))
            return jnp.clip(jnp.round(W / (gamma + EPS)), -1.0, 1.0)
        Wq1 = _quantize(W1)
        Wq2 = _quantize(W2)
        h = jax.nn.relu(jnp.einsum('bsd,fd->bsf', x, Wq1) + b1)
        out = jnp.einsum('bsf,df->bsd', h, Wq2) + b2
        return out
    x = x + jnp.tanh(g_xattn[0]) * _L0_xattn_ref(_layernorm(x, axis=-1), ctx_1024, ctx_1024, L0_xattn_Wi, L0_xattn_bi, L0_xattn_Wg, L0_xattn_bg, L0_xattn_A, L0_xattn_Bm, L0_xattn_Wo, L0_xattn_bo, L0_xattn_decay)
    x = x + jnp.tanh(g_ffn[0]) * _L0_ffn_ref(_layernorm(x, axis=-1), L0_ffn_W1, L0_ffn_b1, L0_ffn_W2, L0_ffn_b2)
    return x

_drawn_inputs = setup_inputs


def setup_inputs(seed=0):
    import zlib

    import numpy as np

    out = dict(_drawn_inputs(seed))
    spreads = {'L0_xattn_decay': (0.8999999761581421, 0.2)}
    factors = {'L0_xattn_bi': 24.025, 'L0_xattn_bg': 37.443, 'L0_ffn_b1': 22.521, 'L0_ffn_b2': 64.0}
    for name, (base, spread) in spreads.items():
        noise = np.random.default_rng([zlib.crc32(name.encode()), seed]).standard_normal(out[name].shape)
        drawn = base * np.exp(spread * noise) if base else spread * noise
        out[name] = jnp.asarray(drawn.astype(out[name].dtype))
    for name, factor in factors.items():
        out[name] = (out[name] * factor).astype(out[name].dtype)
    return out
```

```python
import concourse.bass as bass
from concourse import mybir
from contextlib import ExitStack



def build(nc, x_in, ctx_in, wsq_in, w1_in, w2_in, cols_in, rows_in, out):
    f32 = mybir.dt.float32
    f32r = mybir.dt.float32r
    f16 = mybir.dt.float16
    bf16 = mybir.dt.bfloat16
    i32 = mybir.dt.int32
    ALU = mybir.AluOpType
    ACT = mybir.ActivationFunctionType
    AX = mybir.AxisListType

    P = 128
    NC, _, TILES, D = x_in.shape
    K = D // P
    B = ctx_in.shape[3]
    T = ctx_in.shape[4]
    N = B * T
    F = w1_in.shape[2] // P
    PAIRS = F // 2
    LN_EPS, Q_EPS = 1e-5, 1e-5
    STATE_SCALE = 2.0 ** 4
    OUT_SCALE = 2.0 ** 12
    NORM_SCALE = 2.0 ** 10
    WEIGHT_TOP = 2.0 ** 8
    HIDDEN_TOP = 2.0 ** 13
    HIDDEN_BOUND = float(D)
    assert K == 2 and T * B * K <= 512 and TILES * P == N and F % 2 == 0 and NC % 2 == 0

    C_BI, C_BG, C_DECAY, C_B1 = 0, K, 2 * K, 3 * K
    C_GX, C_GF = 3 * K + F, 3 * K + F + 1
    NCOLS = 3 * K + F + 2
    WI, WG, BM, WA, WO = range(5)

    ctx = ExitStack()
    with ctx:
        def sb(name, shape, dt=f32):
            return ctx.enter_context(nc.sbuf_tensor(name, shape, dt))

        def sem(name):
            return ctx.enter_context(nc.semaphore(name))

        wsq = [sb(f"wsq{n}", [P, K, D]) for n in range(5)]
        wi_hi, wi_lo = sb("wi_hi", [P, K, D], f32r), sb("wi_lo", [P, K, D], f32r)
        wg_hi, wg_lo = sb("wg_hi", [P, K, D], f32r), sb("wg_lo", [P, K, D], f32r)
        bm_hi, bm_lo = sb("bm_hi", [P, K, D], f32r), sb("bm_lo", [P, K, D], f32r)
        aw_hi, aw_lo = sb("aw_hi", [P, K, D], f32r), sb("aw_lo", [P, K, D], f32r)
        wo_scaled = sb("wo_scaled", [P, K, D])
        a_hi, a_lo = sb("a_hi", [P, K, D], f16), sb("a_lo", [P, K, D], f16)
        wo_hi, wo_lo = sb("wo_hi", [P, K, D], f16), sb("wo_lo", [P, K, D], f16)
        w1_raw, w2_raw = sb("w1_raw", [P, K, F * P]), sb("w2_raw", [P, F, D])
        w1_q, w2_q = sb("w1_q", [P, K, F * P], bf16), sb("w2_q", [P, F, D], bf16)
        below = sb("below", [P, 2 * F * D])
        w_abs, unused = sb("w_abs", [P, 4, F * D // 2]), sb("unused", [P, 1])
        cols = sb("cols", [P, NCOLS])
        rows = sb("rows", [P, 2, D])
        bo_g, b2_g = sb("bo_g", [P, D]), sb("b2_g", [P, D])
        b1_s = sb("b1_s", [P, F])
        ident = sb("ident", [P, P])
        ones = sb("ones", [P, P])
        idle = sb("idle", [P, D], bf16)
        minus_half, eps = sb("minus_half", [P, TILES]), sb("eps", [P, TILES])
        mx = sb("mx", [P, 3])
        mx_t = sb("mx_t", [3, 1])
        mx_d = sb("mx_d", [3, 3])
        top = sb("top", [P, 3])
        pow2 = sb("pow2", [P, 3])
        inv = sb("inv", [P, 3])
        sc = sb("sc", [P, 8])
        S_A, S_CH, I_CH, S_WO, S_W1, S_H = (sc[:, n:n + 1] for n in range(6))
        gates = sb("gates", [P, 2])
        gate_sc = sb("gate_sc", [P, 2])
        gsum = sb("gsum", [P, 4])
        gpart = sb("gpart", [P, 2])
        thr = sb("thr", [P, 2])
        thr_n = sb("thr_n", [P, 2])
        x_norm = sb("x_norm", [P, 2, TILES, D])
        x_res = sb("x_res", [P, 2, TILES, D])
        cx = sb("cx", [P, 2, K, B, T])
        cx2 = sb("cx2", [P, K, B, T])
        keep = sb("keep", [P, K, B, T])
        r = sb("r", [P, K, B, T])
        st1, mv1 = sb("st1", [P, TILES, 6]), sb("mv1", [P, TILES, 2])
        ve1, rs1 = sb("ve1", [P, TILES]), sb("rs1", [P, TILES])
        xh1 = sb("xh1", [P, TILES, D])
        ret = sb("ret", [P, K, N])
        ret_hi, ret_lo = sb("ret_hi", [P, K, N], f32r), sb("ret_lo", [P, K, N], f32r)
        inp = sb("inp", [P, K, N])
        inp_hi, inp_lo = sb("inp_hi", [P, K, N], f32r), sb("inp_lo", [P, K, N], f32r)
        rest = sb("rest", [P, K, N])
        rest_hi, rest_lo = sb("rest_hi", [P, K, N], f32r), sb("rest_lo", [P, K, N], f32r)
        gate = sb("gate", [P, 2, K, N])
        state = sb("state", [P, 2, K, N])
        m_hi, m_lo = sb("m_hi", [P, K, B], f16), sb("m_lo", [P, K, B], f16)
        m_all = sb("m_all", [P, K, B])
        s_hi, s_lo = sb("s_hi", [P, K, N], f16), sb("s_lo", [P, K, N], f16)
        x_bo = sb("x_bo", [P, TILES, D])
        x1 = sb("x1", [P, TILES, D])
        x1_b2 = sb("x1_b2", [P, 2, TILES, D])
        st2, mv2 = sb("st2", [P, TILES, 6]), sb("mv2", [P, TILES, 2])
        ve2, rs2 = sb("ve2", [P, TILES]), sb("rs2", [P, TILES])
        xh2 = sb("xh2", [P, TILES, D])
        xt_hi = sb("xt_hi", [P, 2, K, N], f16)
        xt_lo = sb("xt_lo", [P, 2, K, N], f16)
        hid = sb("hid", [P, 2, 2, N])
        h_hi, h_lo = sb("h_hi", [P, F, N], f16), sb("h_lo", [P, F, N], f16)
        y = sb("y", [P, 2, TILES, D])

        def bank(name):
            return ctx.enter_context(nc.psum_tensor(name, [P, 512], f32))

        pre_ps = [bank("pre_ps0"), bank("pre_ps1")]
        ret_ps, inp_ps = bank("ret_ps"), bank("inp_ps")
        hid_ps = [bank("hid_ps0"), bank("hid_ps1")]
        y_ps, att_ps = bank("y_ps"), bank("att_ps")

        cols_in_s, rows_in_s = sem("cols_in_s"), sem("rows_in_s")
        wsq_in_s = [sem(f"wsq_in{n}") for n in range(5)]
        w1_in_s, w2_in_s = sem("w1_in_s"), sem("w2_in_s")
        x_norm_in = [sem("x_norm_in0"), sem("x_norm_in1")]
        x_res_in = [sem("x_res_in0"), sem("x_res_in1")]
        cx_in = [sem("cx_in0"), sem("cx_in1")]
        stored = [sem("stored0"), sem("stored1")]
        const_set = sem("const_set")
        idle_set = sem("idle_set")
        dve_prep = sem("dve_prep")
        act_prep = sem("act_prep")
        pool_prep = sem("pool_prep")
        pe_prep = sem("pe_prep")
        stats1, mean1, vare1, rstd1, xh1_set = (sem(n) for n in ("stats1", "mean1", "vare1", "rstd1", "xh1_set"))
        squared, r_first, r_set = sem("squared"), sem("r_first"), sem("r_set")
        xh1_t = sem("xh1_t")
        ret_set, ret_hi_set, ret_lo_set = sem("ret_set"), sem("ret_hi_set"), sem("ret_lo_set")
        inp_sum, inp_set, inp_hi_set, inp_lo_set = sem("inp_sum"), sem("inp_set"), sem("inp_hi_set"), sem("inp_lo_set")
        gate_sum, gate_set = sem("gate_sum"), sem("gate_set")
        rest_set, rest_hi_set, rest_lo_set = sem("rest_set"), sem("rest_hi_set"), sem("rest_lo_set")
        m_hi_set, m_all_set, m_lo_set = sem("m_hi_set"), sem("m_all_set"), sem("m_lo_set")
        step_sum, state_set = sem("step_sum"), sem("state_set")
        s_hi_set, s_lo_set = sem("s_hi_set"), sem("s_lo_set")
        att_sum, x_bo_set, x1_set, x1_b2_set = sem("att_sum"), sem("x_bo_set"), sem("x1_set"), sem("x1_b2_set")
        stats2, mean2, vare2, rstd2, xh2_set = (sem(n) for n in ("stats2", "mean2", "vare2", "rstd2", "xh2_set"))
        xh2_t, xt_hi_set, xt_lo_set = sem("xh2_t"), sem("xt_hi_set"), sem("xt_lo_set")
        hid_sum, hid_set, h_hi_set, h_lo_set = sem("hid_sum"), sem("hid_set"), sem("h_hi_set"), sem("h_lo_set")
        y_sum, y_set = sem("y_sum"), sem("y_set")

        def number(q):
            return 2 * q[0] + q[1] if isinstance(q[0], int) else q[0] * 2 + q[1]

        def plus(q, d):
            return (q[0], q[1] + d)

        def upto(q, per=1, k=None):
            return number(q) * per + (per if k is None else k)

        def landed(q):
            return q[0] * 16 + (q[1] // 2 + 1) * 16

        def exists(q):
            return not isinstance(q[0], int) or 0 <= q[1] < NC

        HEAD, TAIL = 4, 4
        BODIES = NC + 2
        TURNS = (BODIES - HEAD - TAIL) // 2

        def run(eng, body):
            for n in range(HEAD):
                body((0, n))
            with eng.Fori(0, TURNS) as i:
                for u in range(2):
                    body((i, HEAD + u))
            for n in range(BODIES - TAIL, BODIES):
                body((0, n))

        def stages(c):
            if not isinstance(c[0], int):
                return plus(c, 2), plus(c, 1), c, plus(c, -1), plus(c, -2)
            return tuple(plus(c, d) if exists(plus(c, d)) else None for d in (2, 1, 0, -1, -2))

        TERNARY_AT = {(0, 5): (0,), (0, 6): (1,), (0, 7): (2,), (1, 0): (3,), (1, 1): (4,), (1, 3): (5,),
                      (1, 5): (6,), (1, 7): (7,)}
        HIDDEN_SLOTS = (0, 1, 2, 4)

        def quarter(w, n):
            size = F * D // QUARTERS
            return w[:, :, :].rearrange("p k n -> p (k n)")[:, n * size:(n + 1) * size]

        def below_of(n):
            size = F * D // QUARTERS
            return below[:, n * size:(n + 1) * size]

        def step_cols(j):
            return slice(j * B, (j + 1) * B)

        QUARTERS = 4
        PREP = ["zero", "keep", "mx", "mx_t", "mx_d", "bound", "top", "inv", "s_a", "sc", "a_lo", "bm_lo", "aw_lo", "gates_out",
                "gpart", "gmean", "thr", "thr_n"]
        PREP += [f"sign{n}" for n in range(2 * QUARTERS)]
        done = {name: n + 1 for n, name in enumerate(PREP)}
        PPREP = ["wi", "wg", "wo_scaled", "wo"] + [f"below{n}" for n in range(2 * QUARTERS)]
        pdone = {name: n + 1 for n, name in enumerate(PPREP)}
        APREP = ["gates", "wi", "wg", "a", "bm", "aw", "sums", "wo"]
        APREP += [f"w1_q{n}" for n in range(QUARTERS)]
        adone = {name: n + 1 for n, name in enumerate(APREP)}

        block = ctx.enter_context(nc.Block())

        @block.sync
        def _(sp):
            def load_norm(q):
                if exists(plus(q, -2)):
                    sp.wait_ge(xh1_set, upto(plus(q, -2)))
                    sp.wait_ge(squared, upto(plus(q, -2)))
                sp.dma_start(x_norm[:, q[1] % 2, :, :], x_in[number(q)]).then_inc(x_norm_in[q[1] % 2], 16)
                sp.dma_start(cx[:, q[1] % 2, :, :, :], ctx_in[number(q)]).then_inc(cx_in[q[1] % 2], 16)

            load_norm((0, 0))
            for n in (WA, WG, BM):
                sp.dma_start(wsq[n][:, :, :], wsq_in[n]).then_inc(wsq_in_s[n], 16)
            load_norm((0, 1))
            sp.dma_start(rows[:, :, :], rows_in).then_inc(rows_in_s, 16)
            sp.dma_start(w1_raw[:, :, :], w1_in).then_inc(w1_in_s, 16)
            sp.dma_start(w2_raw[:, :, :], w2_in).then_inc(w2_in_s, 16)

            def store(q):
                sp.wait_ge(y_set, upto(q))
                sp.dma_start(out[number(q)], y[:, q[1] % 2, :, :]).then_inc(stored[q[1] % 2], 16)

            def body(c):
                norm, project, chain, attend, ffn = stages(c)
                if norm:
                    load_norm(norm)
                if chain:
                    if exists(plus(chain, -2)):
                        sp.wait_ge(x_bo_set, upto(plus(chain, -2)))
                    sp.dma_start(x_res[:, c[1] % 2, :, :], x_in[number(chain)]).then_inc(x_res_in[c[1] % 2], 16)
                if exists(plus(c, -3)):
                    store(plus(c, -3))

            run(sp, body)
            store((0, NC - 1))
            for par in range(2):
                sp.wait_ge(stored[par], NC // 2 * 16)

        @block.gpsimd
        def _(pool):
            nc.gpsimd.memset(idle[:, :], 0.0).then_inc(idle_set, 1)
            nc.gpsimd.memset(ident[:, :], 0.0).then_inc(const_set, 1)
            nc.gpsimd.memset(ones[:, :], 1.0).then_inc(const_set, 1)
            nc.gpsimd.memset(minus_half[:, :], -0.5)
            nc.gpsimd.memset(eps[:, :], LN_EPS).then_inc(const_set, 1)
            nc.gpsimd.memset(state[:, 1, :, N - B:N], 0.0).then_inc(const_set, 1)
            pool.wait_ge(const_set, 4)
            nc.gpsimd.affine_select(out=ident[:, :], in_=ident[:, :], compare_op=ALU.not_equal, fill=1.0,
                                    base=0, pattern=[[-1, P]], channel_multiplier=1).then_inc(const_set, 1)

            def rstd1_of(q):
                pool.wait_ge(mean1, upto(q))
                nc.gpsimd.tensor_tensor(ve1[:, :], mv1[:, :, 1], eps[:, :], ALU.add).then_inc(vare1, 1)
                pool.wait_ge(vare1, upto(q))
                if exists(plus(q, -1)):
                    pool.wait_ge(xh1_set, upto(plus(q, -1)))
                nc.gpsimd.tensor_tensor(rs1[:, :], ve1[:, :], minus_half[:, :], ALU.pow).then_inc(rstd1, 1)

            def low(name, whole, high, part):
                pool.wait_ge(act_prep, adone[name])
                high = high[:, :, :] if high.dtype == f16 else high[:, :, :].bitcast(f32)
                nc.gpsimd.tensor_tensor(part[:, :, :], whole[:, :, :], high, ALU.subtract).then_inc(pool_prep, 1)

            rstd1_of((0, 0))
            low("wi", wsq[WI], wi_hi, wi_lo)
            low("wg", wsq[WG], wg_hi, wg_lo)
            rstd1_of((0, 1))
            pool.wait_ge(dve_prep, done["sc"])
            nc.gpsimd.tensor_scalar(wo_scaled[:, :, :], wsq[WO][:, :, :], S_WO, None, ALU.mult).then_inc(pool_prep, 1)
            pool.wait_ge(pool_prep, pdone["wo_scaled"])

            def find_below(lo, hi):
                pool.wait_ge(dve_prep, done["thr_n"])
                for n in range(lo, hi):
                    w, piece = n // QUARTERS, n % QUARTERS
                    nc.gpsimd.tensor_scalar(below_of(n), quarter((w1_raw, w2_raw)[w], piece), thr_n[:, w:w + 1],
                                            None, ALU.is_lt).then_inc(pool_prep, 1)

            def body(c):
                norm, project, chain, attend, ffn = stages(c)
                if attend:
                    pool.wait_ge(x_res_in[attend[1] % 2], landed(attend))
                    if isinstance(c[0], int) and c[1] == 1:
                        pool.wait_ge(dve_prep, done["gates_out"])
                    if exists(plus(attend, -1)):
                        pool.wait_ge(x1_set, upto(plus(attend, -1)))
                    nc.gpsimd.tensor_tensor(x_bo[:, :, :], x_res[:, attend[1] % 2, :, :],
                                            bo_g[:, :].unsqueeze(1).to_broadcast([P, TILES, D]), ALU.add).then_inc(x_bo_set, 1)
                if norm:
                    rstd1_of(norm)
                if isinstance(c[0], int) and c[1] == 0:
                    low("wo", wo_scaled, wo_hi, wo_lo)
                    find_below(0, 6)
                if isinstance(c[0], int) and c[1] == 1:
                    find_below(6, 8)
                if attend:
                    pool.wait_ge(mean2, upto(attend))
                    nc.gpsimd.tensor_tensor(ve2[:, :], mv2[:, :, 1], eps[:, :], ALU.add).then_inc(vare2, 1)
                    pool.wait_ge(vare2, upto(attend))
                    nc.gpsimd.tensor_tensor(rs2[:, :], ve2[:, :], minus_half[:, :], ALU.pow).then_inc(rstd2, 1)
                    if exists(plus(attend, -2)):
                        pool.wait_ge(y_set, upto(plus(attend, -2)))
                    nc.gpsimd.tensor_tensor(x1_b2[:, attend[1] % 2, :, :], x1[:, :, :],
                                            b2_g[:, :].unsqueeze(1).to_broadcast([P, TILES, D]), ALU.add).then_inc(x1_b2_set, 1)

            run(pool, body)

        @block.scalar
        def _(act):
            act.dma_start(wsq[WI][:, :, :], wsq_in[WI]).then_inc(wsq_in_s[WI], 16)
            act.dma_start(cols[:, :], cols_in).then_inc(cols_in_s, 16)
            act.dma_start(wsq[WO][:, :, :], wsq_in[WO]).then_inc(wsq_in_s[WO], 16)
            act.wait_ge(const_set, 4)
            nc.scalar.activation(unused[:, :], ones[:, 0:1], ACT.Sigmoid)
            act.wait_ge(cols_in_s, 16)
            nc.scalar.activation(gates[:, :], cols[:, C_GX:C_GX + 2], ACT.Tanh).then_inc(act_prep, 1)

            def square(q):
                act.wait_ge(cx_in[q[1] % 2], landed(q))
                if exists(plus(q, -1)):
                    act.wait_ge(r_set, upto(plus(q, -1)))
                nc.scalar.activation(cx2[:, :, :, :], cx[:, q[1] % 2, :, :, :], ACT.Square).then_inc(squared, 1)

            square((0, 0))
            act.wait_ge(wsq_in_s[WI], 16)
            nc.scalar.copy(wi_hi[:, :, :], wsq[WI][:, :, :]).then_inc(act_prep, 1)
            act.wait_ge(wsq_in_s[WG], 16)
            nc.scalar.copy(wg_hi[:, :, :], wsq[WG][:, :, :]).then_inc(act_prep, 1)
            def ret_high(q):
                act.wait_ge(ret_set, upto(q))
                nc.scalar.copy(ret_hi[:, :, :], ret[:, :, :]).then_inc(ret_hi_set, 1)

            def inp_out(q):
                act.wait_ge(inp_sum, upto(q))
                for m in range(K):
                    last = nc.scalar.activation(inp[:, m, :], inp_ps[:, m * N:(m + 1) * N], ACT.Identity,
                                                bias=cols[:, C_BI + m:C_BI + m + 1])
                last.then_inc(inp_set, 1)
                act.wait_ge(inp_set, upto(q))
                nc.scalar.copy(inp_hi[:, :, :], inp[:, :, :]).then_inc(inp_hi_set, 1)

            def gate_out(q):
                act.wait_ge(gate_sum, upto(q))
                for m in range(K):
                    last = nc.scalar.activation(gate[:, q[1] % 2, m, :], ret_ps[:, m * N:(m + 1) * N], ACT.Sigmoid,
                                                bias=cols[:, C_BG + m:C_BG + m + 1])
                last.then_inc(gate_set, 1)

            def rest_high(q):
                act.wait_ge(rest_set, upto(q))
                nc.scalar.copy(rest_hi[:, :, :], rest[:, :, :]).then_inc(rest_hi_set, 1)

            def state_high(q):
                act.wait_ge(state_set, upto(q, T))
                nc.scalar.mul(s_hi[:, :, :], state[:, q[1] % 2, :, :], OUT_SCALE).then_inc(s_hi_set, 1)

            def normed_high(q):
                act.wait_ge(xh2_t, upto(q))
                nc.scalar.mul(xt_hi[:, q[1] % 2, :, :], att_ps[:, :].rearrange("p (k n) -> p k n", k=K), NORM_SCALE).then_inc(xt_hi_set, 1)

            def hidden(q, p):
                act.wait_ge(hid_sum, upto(q, PAIRS, p + 1))
                if p >= 2:
                    act.wait_ge(h_lo_set, upto(q, PAIRS, p - 1))
                elif exists(plus(q, -1)):
                    act.wait_ge(h_lo_set, upto(plus(q, -1), PAIRS, PAIRS + p - 1))
                for u in range(2):
                    last = nc.scalar.activation(hid[:, p % 2, u, :], hid_ps[p % 2][:, u * N:(u + 1) * N], ACT.Relu,
                                                bias=b1_s[:, 2 * p + u:2 * p + u + 1])
                last.then_inc(hid_set, 1)

            def hidden_high(q, p):
                act.wait_ge(hid_set, upto(q, PAIRS, p + 1))
                nc.scalar.copy(h_hi[:, 2 * p:2 * p + 2, :], hid[:, p % 2, :, :]).then_inc(h_hi_set, 1)

            def tanh_step(q, j):
                act.wait_ge(step_sum, upto(q, T, j + 1))
                nc.scalar.activation(state[:, q[1] % 2, :, step_cols(j)],
                                     pre_ps[q[1] % 2][:, :].rearrange("p (k n) -> p k n", k=K)[:, :, step_cols(j)],
                                     ACT.Tanh, scale=I_CH).then_inc(state_set, 1)

            def half_sum(n):
                w = (w1_raw[:, :, :].rearrange("p k n -> p (k n)") if n < 2 else
                     w2_raw[:, :, :].rearrange("p f n -> p (f n)"))
                act.wait_ge(w1_in_s if n < 2 else w2_in_s, 16)
                size = F * D // 2
                return nc.scalar.activation(w_abs[:, n, :], w[:, n % 2 * size:(n % 2 + 1) * size], ACT.Abs,
                                            accum_out=gsum[:, n:n + 1])

            def scaled_high(high, weight, by):
                act.wait_ge(wsq_in_s[weight], 16)
                nc.scalar.mul(high[:, :, :], wsq[weight][:, :, :], by).then_inc(act_prep, 1)

            ret_high((0, 0))
            square((0, 1))
            act.wait_ge(dve_prep, done["s_a"])
            scaled_high(a_hi, WA, S_A)
            inp_out((0, 0))
            act.wait_ge(dve_prep, done["sc"])
            scaled_high(bm_hi, BM, S_CH)
            scaled_high(aw_hi, WA, S_CH)
            gate_out((0, 0))
            rest_high((0, 0))
            half_sum(0)
            half_sum(1)

            def body(c):
                norm, project, chain, attend, ffn = stages(c)
                peeled = c[1] if isinstance(c[0], int) else None
                if attend:
                    state_high(attend)
                for j in range(T):
                    if chain:
                        tanh_step(chain, j)
                    if j == 1 and project:
                        ret_high(project)
                    if j in HIDDEN_SLOTS and ffn:
                        hidden(ffn, HIDDEN_SLOTS.index(j))
                        hidden_high(ffn, HIDDEN_SLOTS.index(j))
                    if j == 3 and project:
                        inp_out(project)
                    if j == 5:
                        if project:
                            gate_out(project)
                        if norm:
                            square(norm)
                    if j == 6:
                        if project:
                            rest_high(project)
                        if attend:
                            normed_high(attend)
                    if peeled == 0:
                        if j == 0:
                            half_sum(2)
                        if j == 1:
                            half_sum(3).then_inc(act_prep, 1)
                        if j == 2:
                            scaled_high(wo_hi, WO, S_WO)
                    for n in TERNARY_AT.get((peeled, j - 1) if j else (None if peeled is None else peeled - 1, T - 1), ()):
                        if n < QUARTERS:
                            act.wait_ge(dve_prep, done[f"sign{n}"])
                            nc.scalar.mul(quarter(w1_q, n), quarter(w1_raw, n), S_W1).then_inc(act_prep, 1)

            run(act, body)

        @block.vector
        def _(dve):
            def prep(name, ins):
                ins.then_inc(dve_prep, 1)
                dve.wait_ge(dve_prep, done[name])

            def norm_stats(q):
                dve.wait_ge(x_norm_in[q[1] % 2], landed(q))
                for t in range(TILES):
                    last = nc.vector.bn_stats(st1[:, t, :], x_norm[:, q[1] % 2, t, :])
                last.then_inc(stats1, 1)
                dve.wait_ge(stats1, upto(q))

            def norm_mean(q):
                for t in range(TILES):
                    last = nc.vector.bn_aggr(mv1[:, t, :], st1[:, t, :])
                last.then_inc(mean1, 1)

            def norm_apply(q):
                dve.wait_ge(rstd1, upto(q))
                if exists(plus(q, -1)):
                    dve.wait_ge(xh1_t, upto(plus(q, -1)))
                for t in range(TILES):
                    last = nc.vector.tensor_scalar(xh1[:, t, :], x_norm[:, q[1] % 2, t, :], mv1[:, t, 0:1],
                                                   rs1[:, t:t + 1], ALU.subtract, ALU.mult)
                last.then_inc(xh1_set, 1)

            def scan(q):
                dve.wait_ge(squared, upto(q))
                if exists(plus(q, -1)):
                    for k in range(K):
                        last = nc.vector.scalar_tensor_tensor(
                            out=cx2[:, k, :, 0], in0=r[:, k, :, T - 1], scalar=cols[:, C_DECAY + k:C_DECAY + k + 1],
                            in1=cx2[:, k, :, 0], op0=ALU.mult, op1=ALU.add)
                    last.then_inc(r_first, 1)
                    dve.wait_ge(r_first, upto(plus(q, -1)))
                nc.vector.tensor_tensor_scan(r[:, :, :, :].rearrange("p k b t -> p (k b t)"),
                                             keep[:, :, :, :].rearrange("p k b t -> p (k b t)"),
                                             cx2[:, :, :, :].rearrange("p k b t -> p (k b t)"),
                                             0.0, ALU.mult, ALU.add).then_inc(r_set, 1)

            def retain(q):
                dve.wait_ge(xh1_t, upto(q))
                dve.wait_ge(r_set, upto(q))
                nc.vector.tensor_tensor(ret[:, :, :].rearrange("p k (t b) -> p k t b", t=T),
                                        ret_ps[:, :].rearrange("p (k t b) -> p k t b", k=K, t=T),
                                        r[:, :, :, :].rearrange("p k b t -> p k t b"), ALU.mult).then_inc(ret_set, 1)

            def ret_low(q):
                dve.wait_ge(ret_hi_set, upto(q))
                nc.vector.tensor_tensor(ret_lo[:, :, :], ret[:, :, :], ret_hi[:, :, :].bitcast(f32),
                                        ALU.subtract).then_inc(ret_lo_set, 1)

            def inp_low(q):
                dve.wait_ge(inp_hi_set, upto(q))
                nc.vector.tensor_tensor(inp_lo[:, :, :], inp[:, :, :], inp_hi[:, :, :].bitcast(f32),
                                        ALU.subtract).then_inc(inp_lo_set, 1)

            def rest_all(q):
                dve.wait_ge(gate_set, upto(q))
                nc.vector.scalar_tensor_tensor(out=rest[:, :, :], in0=gate[:, q[1] % 2, :, :], scalar=1.0,
                                               in1=inp[:, :, :], op0=ALU.subtract, op1=ALU.mult,
                                               reverse0=True).then_inc(rest_set, 1)

            def rest_low(q):
                dve.wait_ge(rest_hi_set, upto(q))
                nc.vector.tensor_tensor(rest_lo[:, :, :], rest[:, :, :], rest_hi[:, :, :].bitcast(f32),
                                        ALU.subtract).then_inc(rest_lo_set, 1)

            def gated_state(q, j):
                par = q[1] % 2
                if j == 0:
                    dve.wait_ge(gate_set, upto(q))
                    before = state[:, 1 - par, :, step_cols(T - 1)]
                    if exists(plus(q, -1)):
                        dve.wait_ge(state_set, upto(plus(q, -1), T))
                    else:
                        dve.wait_ge(const_set, 4)
                else:
                    before = state[:, par, :, step_cols(j - 1)]
                    dve.wait_ge(state_set, upto(q, T, j))
                now = gate[:, par, :, step_cols(j)]
                nc.vector.scalar_tensor_tensor(out=m_hi[:, :, :], in0=before, scalar=STATE_SCALE, in1=now,
                                               op0=ALU.mult, op1=ALU.mult).then_inc(m_hi_set, 1)
                nc.vector.scalar_tensor_tensor(out=m_all[:, :, :], in0=before, scalar=STATE_SCALE, in1=now,
                                               op0=ALU.mult, op1=ALU.mult).then_inc(m_all_set, 1)
                dve.wait_ge(m_all_set, upto(q, T, j + 1))
                nc.vector.tensor_tensor(m_lo[:, :, :], m_all[:, :, :], m_hi[:, :, :], ALU.subtract).then_inc(m_lo_set, 1)

            def state_low(q):
                dve.wait_ge(s_hi_set, upto(q))
                nc.vector.scalar_tensor_tensor(out=s_lo[:, :, :], in0=state[:, q[1] % 2, :, :], scalar=OUT_SCALE,
                                               in1=s_hi[:, :, :], op0=ALU.mult, op1=ALU.subtract).then_inc(s_lo_set, 1)

            def residual(q):
                dve.wait_ge(x_bo_set, upto(q))
                if exists(plus(q, -1)):
                    dve.wait_ge(x1_b2_set, upto(plus(q, -1)))
                dve.wait_ge(att_sum, upto(q))
                nc.vector.scalar_tensor_tensor(out=x1[:, :, :], in0=att_ps[:, :].rearrange("p (t d) -> p t d", t=TILES),
                                               scalar=gate_sc[:, 0:1], in1=x_bo[:, :, :],
                                               op0=ALU.mult, op1=ALU.add).then_inc(x1_set, 1)

            def x1_stats(q):
                dve.wait_ge(x1_set, upto(q))
                for t in range(TILES):
                    last = nc.vector.bn_stats(st2[:, t, :], x1[:, t, :])
                last.then_inc(stats2, 1)
                dve.wait_ge(stats2, upto(q))

            def x1_mean(q):
                for t in range(TILES):
                    last = nc.vector.bn_aggr(mv2[:, t, :], st2[:, t, :])
                last.then_inc(mean2, 1)

            def x1_apply(q):
                dve.wait_ge(rstd2, upto(q))
                for t in range(TILES):
                    last = nc.vector.tensor_scalar(xh2[:, t, :], x1[:, t, :], mv2[:, t, 0:1], rs2[:, t:t + 1],
                                                   ALU.subtract, ALU.mult)
                last.then_inc(xh2_set, 1)

            def normed_low(q):
                dve.wait_ge(xt_hi_set, upto(q))
                nc.vector.scalar_tensor_tensor(out=xt_lo[:, q[1] % 2, :, :], in0=att_ps[:, :].rearrange("p (k n) -> p k n", k=K),
                                               scalar=NORM_SCALE, in1=xt_hi[:, q[1] % 2, :, :],
                                               op0=ALU.mult, op1=ALU.subtract).then_inc(xt_lo_set, 1)

            def hidden_low(q, p):
                dve.wait_ge(h_hi_set, upto(q, PAIRS, p + 1))
                nc.vector.tensor_tensor(h_lo[:, 2 * p:2 * p + 2, :], hid[:, p % 2, :, :],
                                        h_hi[:, 2 * p:2 * p + 2, :], ALU.subtract).then_inc(h_lo_set, 1)

            def finish(q):
                dve.wait_ge(x1_b2_set, upto(q))
                if exists(plus(q, -2)):
                    dve.wait_ge(stored[q[1] % 2], landed(plus(q, -2)))
                dve.wait_ge(y_sum, upto(q))
                nc.vector.scalar_tensor_tensor(out=y[:, q[1] % 2, :, :], in0=y_ps[:, :].rearrange("p (t d) -> p t d", t=TILES),
                                               scalar=gate_sc[:, 1:2], in1=x1_b2[:, q[1] % 2, :, :],
                                               op0=ALU.mult, op1=ALU.add).then_inc(y_set, 1)

            def scaled_low(name, high, part, weight, by):
                dve.wait_ge(act_prep, adone[name])
                high = high[:, :, :] if high.dtype == f16 else high[:, :, :].bitcast(f32)
                prep(f"{name}_lo", nc.vector.scalar_tensor_tensor(out=part[:, :, :], in0=wsq[weight][:, :, :],
                                                                  scalar=by, in1=high, op0=ALU.mult,
                                                                  op1=ALU.subtract))

            prep("zero", nc.vector.memset(keep[:, :, :, :], 0.0))
            norm_stats((0, 0))
            norm_mean((0, 0))
            dve.wait_ge(cols_in_s, 16)
            for k in range(K):
                last = nc.vector.tensor_scalar(keep[:, k, :, 1:T], keep[:, k, :, 1:T],
                                               cols[:, C_DECAY + k:C_DECAY + k + 1], None, ALU.add)
            prep("keep", last)

            scan((0, 0))
            norm_apply((0, 0))
            nc.vector.tensor_reduce(mx[:, 2:3], cols[:, C_B1:C_B1 + F], AX.X, ALU.max, apply_absolute_value=True)
            dve.wait_ge(wsq_in_s[WA], 16)
            nc.vector.tensor_reduce(mx[:, 0:1], wsq[WA][:, :, :], AX.XY, ALU.max, apply_absolute_value=True)
            dve.wait_ge(wsq_in_s[WO], 16)
            prep("mx", nc.vector.tensor_reduce(mx[:, 1:2], wsq[WO][:, :, :], AX.XY, ALU.max, apply_absolute_value=True))
            retain((0, 0))
            dve.wait_ge(pe_prep, 1)
            prep("mx_t", nc.vector.tensor_reduce(mx_t[:, :], att_ps[0:3, 0:P], AX.X, ALU.max))
            prep("mx_d", nc.vector.tensor_scalar(mx_d[:, :], ident[0:3, 0:3], mx_t[:, :], None, ALU.mult))
            ret_low((0, 0))
            dve.wait_ge(pe_prep, 2)
            nc.vector.tensor_scalar(top[:, 0:2], y_ps[:, 0:2], 2.0 ** -60, None, ALU.max)
            prep("bound", nc.vector.tensor_scalar(top[:, 2:3], y_ps[:, 2:3], HIDDEN_BOUND, None, ALU.add))
            prep("top", nc.vector.tensor_scalar(pow2[:, :].bitcast(i32), top[:, :].bitcast(i32), 0x7F800000, None,
                                                ALU.bitwise_and))
            prep("inv", nc.vector.reciprocal(inv[:, :], pow2[:, :]))
            prep("s_a", nc.vector.tensor_scalar(S_A, inv[:, 0:1], WEIGHT_TOP, None, ALU.mult))
            nc.vector.tensor_scalar(S_CH, inv[:, 0:1], WEIGHT_TOP * STATE_SCALE, None, ALU.mult)
            nc.vector.tensor_scalar(I_CH, pow2[:, 0:1], 1.0 / (WEIGHT_TOP * STATE_SCALE), None, ALU.mult)
            nc.vector.tensor_scalar(S_WO, inv[:, 1:2], WEIGHT_TOP, None, ALU.mult)
            nc.vector.tensor_scalar(S_W1, inv[:, 2:3], HIDDEN_TOP / NORM_SCALE, None, ALU.mult)
            prep("sc", nc.vector.tensor_scalar(S_H, inv[:, 2:3], HIDDEN_TOP, None, ALU.mult))
            norm_stats((0, 1))
            norm_mean((0, 1))
            scaled_low("a", a_hi, a_lo, WA, S_A)
            inp_low((0, 0))
            scaled_low("bm", bm_hi, bm_lo, BM, S_CH)
            scaled_low("aw", aw_hi, aw_lo, WA, S_CH)
            dve.wait_ge(act_prep, adone["gates"])
            nc.vector.tensor_scalar(gate_sc[:, 0:1], pow2[:, 1:2], 1.0 / (WEIGHT_TOP * OUT_SCALE), gates[:, 0:1],
                                    ALU.mult, ALU.mult)
            nc.vector.tensor_scalar(gate_sc[:, 1:2], pow2[:, 2:3], 1.0 / HIDDEN_TOP, gates[:, 1:2], ALU.mult, ALU.mult)
            nc.vector.tensor_scalar(b1_s[:, :], cols[:, C_B1:C_B1 + F], S_H, None, ALU.mult)
            dve.wait_ge(rows_in_s, 16)
            nc.vector.tensor_scalar(b2_g[:, :], rows[:, 1, :], gates[:, 1:2], None, ALU.mult)
            prep("gates_out", nc.vector.tensor_scalar(bo_g[:, :], rows[:, 0, :], gates[:, 0:1], None, ALU.mult))
            norm_apply((0, 1))
            rest_all((0, 0))
            scan((0, 1))
            rest_low((0, 0))

            def sums_of_partition():
                dve.wait_ge(act_prep, adone["sums"])
                prep("gpart", nc.vector.tensor_reduce(gpart[:, :], gsum[:, :].rearrange("p (w h) -> p w h", w=2),
                                                                  AX.X, ALU.add))

            def threshold():
                dve.wait_ge(pe_prep, 3)
                prep("gmean", nc.vector.tensor_scalar(thr[:, :], y_ps[:, 0:2], 1.0 / (F * P * D), Q_EPS,
                                                      ALU.mult, ALU.add))
                prep("thr", nc.vector.tensor_scalar(thr[:, :], thr[:, :], 0.5, None, ALU.mult))
                prep("thr_n", nc.vector.tensor_scalar(thr_n[:, :], thr[:, :], -1.0, None, ALU.mult))

            def ternary(n):
                w, piece = n // QUARTERS, n % QUARTERS
                raw = quarter((w1_raw, w2_raw)[w], piece)
                dve.wait_ge(pool_prep, pdone[f"below{n}"])
                prep(f"sign{n}", nc.vector.scalar_tensor_tensor(out=quarter((w1_raw, w2_q)[w], piece), in0=raw,
                                                                scalar=thr[:, w:w + 1], in1=below_of(n),
                                                                op0=ALU.is_gt, op1=ALU.subtract))

            def body(c):
                norm, project, chain, attend, ffn = stages(c)
                peeled = c[1] if isinstance(c[0], int) else None
                for j in range(T):
                    if chain:
                        gated_state(chain, j)
                    if j == 0:
                        if norm:
                            norm_stats(norm)
                        if attend:
                            state_low(attend)
                        if norm:
                            norm_mean(norm)
                    if j == 1:
                        if project:
                            retain(project)
                        if ffn:
                            hidden_low(ffn, 0)
                    if j == 2:
                        if project:
                            ret_low(project)
                        if attend:
                            residual(attend)
                    if j == 3:
                        if attend:
                            x1_stats(attend)
                        if ffn:
                            hidden_low(ffn, 1)
                        if attend:
                            x1_mean(attend)
                    if j == 4:
                        if project:
                            inp_low(project)
                        if norm:
                            norm_apply(norm)
                        if ffn:
                            hidden_low(ffn, 2)
                    if j == 5:
                        if attend:
                            x1_apply(attend)
                        if ffn:
                            hidden_low(ffn, 3)
                    if j == 6:
                        if project:
                            rest_all(project)
                        if norm:
                            scan(norm)
                    if j == 7:
                        if project:
                            rest_low(project)
                        if attend:
                            normed_low(attend)
                        if ffn:
                            finish(ffn)
                    if peeled == 0:
                        if j == 2:
                            sums_of_partition()
                        if j == 3:
                            threshold()
                    for n in TERNARY_AT.get((peeled, j), ()):
                        ternary(n)

            run(dve, body)

        @block.tensor
        def _(pe):
            def parts(out_of, w_hi, w_lo, v_hi, v_lo, start=True, stop=True, blocks=range(K)):
                for m in blocks:
                    cut = slice(m * P, (m + 1) * P)
                    terms = [(w, v, k) for k in range(K) for w, v in ((w_hi, v_hi), (w_hi, v_lo), (w_lo, v_hi))]
                    for n, (w, v, k) in enumerate(terms):
                        last = nc.tensor.matmul(out_of(m), w[:, k, cut], v[:, k, :],
                                                start=start and n == 0 and (m == 0 or stop),
                                                stop=stop and n == len(terms) - 1,
                                                skip_group_check=not stop or not start)
                return last

            def normed_t(q):
                pe.wait_ge(xh1_set, upto(q))
                for t in range(TILES):
                    for k in range(K):
                        last = nc.tensor.transpose(ret_ps[:, k * N + t * P:k * N + (t + 1) * P],
                                                   xh1[:, t, k * P:(k + 1) * P], ident[:, :])
                last.then_inc(xh1_t, 1)

            def inp_product(q):
                pe.wait_ge(ret_lo_set, upto(q))
                parts(lambda m: inp_ps[:, m * N:(m + 1) * N], wi_hi, wi_lo, ret_hi, ret_lo).then_inc(inp_sum, 1)

            def gate_product(q):
                pe.wait_ge(inp_lo_set, upto(q))
                parts(lambda m: ret_ps[:, m * N:(m + 1) * N], wg_hi, wg_lo, inp_hi, inp_lo).then_inc(gate_sum, 1)

            def from_inp(q, m):
                if m == 0 and exists(plus(q, -2)):
                    pe.wait_ge(state_set, upto(plus(q, -2), T))
                parts(lambda m: pre_ps[q[1] % 2][:, m * N:(m + 1) * N], bm_hi, bm_lo, inp_hi, inp_lo,
                      start=True, stop=False, blocks=(m,))

            def from_rest(q):
                pe.wait_ge(rest_lo_set, upto(q))
                parts(lambda m: pre_ps[q[1] % 2][:, m * N:(m + 1) * N], aw_hi, aw_lo, rest_hi, rest_lo,
                      start=False, stop=False)

            def step(q, j):
                pe.wait_ge(m_hi_set, upto(q, T, j + 1))
                for m in range(K):
                    for k in range(K):
                        for w in (a_hi, a_lo):
                            nc.tensor.matmul(pre_ps[q[1] % 2][:, m * N + j * B:m * N + (j + 1) * B],
                                             w[:, k, m * P:(m + 1) * P], m_hi[:, k, :],
                                             start=False, stop=False, skip_group_check=True)
                pe.wait_ge(m_lo_set, upto(q, T, j + 1))
                for m in range(K):
                    for k in range(K):
                        last = nc.tensor.matmul(pre_ps[q[1] % 2][:, m * N + j * B:m * N + (j + 1) * B],
                                                a_hi[:, k, m * P:(m + 1) * P], m_lo[:, k, :],
                                                start=False, stop=k == K - 1, skip_group_check=True)
                last.then_inc(step_sum, 1)

            def output_product(q, t):
                if t == 0:
                    pe.wait_ge(s_lo_set, upto(q))
                cut = slice(t * P, (t + 1) * P)
                terms = [(s, w, k) for k in range(K) for s, w in ((s_hi, wo_hi), (s_hi, wo_lo), (s_lo, wo_hi))]
                for n, (s, w, k) in enumerate(terms):
                    last = nc.tensor.matmul(att_ps[:, t * D:(t + 1) * D], s[:, k, cut], w[:, k, :],
                                            start=n == 0, stop=n == len(terms) - 1)
                if t == TILES - 1:
                    last.then_inc(att_sum, 1)

            def x1_t(q):
                pe.wait_ge(xh2_set, upto(q))
                for t in range(TILES):
                    for k in range(K):
                        last = nc.tensor.transpose(att_ps[:, k * N + t * P:k * N + (t + 1) * P],
                                                   xh2[:, t, k * P:(k + 1) * P], ident[:, :])
                last.then_inc(xh2_t, 1)

            def hidden_product(q, p):
                if p == 0:
                    pe.wait_ge(xt_lo_set, upto(q))
                if p >= 2:
                    pe.wait_ge(hid_set, upto(q, PAIRS, p - 1))
                elif exists(plus(q, -1)):
                    pe.wait_ge(hid_set, upto(plus(q, -1), PAIRS, PAIRS + p - 1))
                par = q[1] % 2
                for u in range(2):
                    cut = slice((2 * p + u) * P, (2 * p + u + 1) * P)
                    terms = [(v, k) for k in range(K) for v in (xt_hi, xt_lo)]
                    for n, (v, k) in enumerate(terms):
                        last = nc.tensor.matmul(hid_ps[p % 2][:, u * N:(u + 1) * N], w1_q[:, k, cut], v[:, par, k, :],
                                                start=n == 0, stop=n == len(terms) - 1)
                last.then_inc(hid_sum, 1)

            def y_product(q, f):
                if f == 0 and exists(plus(q, -1)):
                    pe.wait_ge(y_set, upto(plus(q, -1)))
                pe.wait_ge(h_lo_set, upto(q, PAIRS, f // 2 + 1))
                for t in range(TILES):
                    for h in (h_hi, h_lo):
                        last = nc.tensor.matmul(y_ps[:, t * D:(t + 1) * D], h[:, f, t * P:(t + 1) * P], w2_q[:, f, :],
                                                start=f == 0 and t == 0 and h is h_hi,
                                                stop=f == F - 1 and h is h_lo, skip_group_check=True)
                if f == F - 1:
                    last.then_inc(y_sum, 1)

            def keep_warm(n):
                for _ in range(n):
                    nc.tensor.matmul(hid_ps[1][:, 0:D], idle[:, 0:P], idle[:, :], start=True, stop=True)

            WARM = {"start": 38, "mx": 6, "top": 4, "inp": 16, "bm": 8}
            WARM_STEP = (6, 4)
            pe.wait_ge(idle_set, 1)
            keep_warm(WARM["start"])
            pe.wait_ge(const_set, 5)
            normed_t((0, 0))
            pe.wait_ge(dve_prep, done["mx"])
            nc.tensor.transpose(att_ps[0:3, 0:P], mx[:, :], ident[:, :]).then_inc(pe_prep, 1)
            keep_warm(WARM["mx"])
            pe.wait_ge(dve_prep, done["mx_d"])
            nc.tensor.matmul(y_ps[:, 0:3], ones[0:3, :], mx_d[:, :], start=True, stop=True).then_inc(pe_prep, 1)
            keep_warm(WARM["top"])
            pe.wait_ge(pool_prep, pdone["wi"])
            inp_product((0, 0))
            keep_warm(WARM["inp"])
            pe.wait_ge(pool_prep, pdone["wg"])
            gate_product((0, 0))
            pe.wait_ge(dve_prep, done["bm_lo"])
            from_inp((0, 0), 0)
            from_inp((0, 0), 1)
            keep_warm(WARM["bm"])
            pe.wait_ge(dve_prep, done["aw_lo"])
            from_rest((0, 0))

            def body(c):
                norm, project, chain, attend, ffn = stages(c)
                peeled = c[1] if isinstance(c[0], int) else None
                for j in range(T):
                    if chain:
                        step(chain, j)
                    if ffn and j < PAIRS:
                        if peeled == 2 and j == 0:
                            pe.wait_ge(act_prep, adone[f"w1_q{QUARTERS - 1}"])
                        hidden_product(ffn, j)
                    if j == 0 and project:
                        normed_t(project)
                    if j < TILES and attend:
                        if peeled == 1 and j == 0:
                            pe.wait_ge(pool_prep, pdone["wo"])
                        output_product(attend, j)
                    if j == 2 and project:
                        inp_product(project)
                    if j == 4 and project:
                        gate_product(project)
                    if ffn:
                        if peeled == 2 and j == 3:
                            pe.wait_ge(dve_prep, done[f"sign{2 * QUARTERS - 1}"])
                        for f in {3: (0, 1), 4: (2,), 5: (3, 4, 5), 6: (6, 7)}.get(j, ()):
                            y_product(ffn, f)
                    if j == 5 and attend:
                        x1_t(attend)
                    if project:
                        if j == 6:
                            from_inp(project, 0)
                        if j == 7:
                            from_inp(project, 1)
                            from_rest(project)
                    if peeled == 0 and j == 2:
                        pe.wait_ge(dve_prep, done["gpart"])
                        nc.tensor.matmul(y_ps[:, 0:2], ones[:, :], gpart[:, :], start=True,
                                         stop=True).then_inc(pe_prep, 1)
                    if peeled in (0, 1):
                        keep_warm(WARM_STEP[peeled])

            run(pe, body)


def kernel(x, ctx_1024, g_xattn, g_ffn, L0_xattn_Wi, L0_xattn_bi, L0_xattn_Wg, L0_xattn_bg, L0_xattn_A,
           L0_xattn_Bm, L0_xattn_Wo, L0_xattn_bo, L0_xattn_decay, L0_ffn_W1, L0_ffn_b1, L0_ffn_W2, L0_ffn_b2):
    import numpy as np
    import concourse.bacc as bacc
    from concourse.bass_utils import run_bass_kernel_spmd

    P, T = 128, 8
    x, ctx = np.asarray(x), np.asarray(ctx_1024)
    B, S, D = x.shape
    NC, K, TILES = S // T, D // P, T * B // P
    STEPS = T // TILES

    def lhs_t(w):
        t = np.asarray(w).T
        return np.ascontiguousarray(t.reshape(t.shape[0] // P, P, t.shape[1]).transpose(1, 0, 2))

    def column(v):
        return np.asarray(v).reshape(-1, P).T

    decay = np.repeat(np.asarray(L0_xattn_decay).reshape(-1), D // L0_xattn_decay.shape[1])
    gates = np.broadcast_to(np.concatenate([np.asarray(g_xattn), np.asarray(g_ffn)])[None, :], (P, 2))
    arrays = {
        "x_in": x.reshape(B, NC, TILES, STEPS, D).transpose(1, 3, 0, 2, 4).reshape(NC, P, TILES, D),
        "ctx_in": ctx.reshape(B, NC, T, K, P).transpose(1, 4, 3, 0, 2),
        "wsq_in": np.stack([lhs_t(w) for w in (L0_xattn_Wi, L0_xattn_Wg, L0_xattn_Bm, L0_xattn_A, L0_xattn_Wo)]),
        "w1_in": lhs_t(L0_ffn_W1),
        "w2_in": lhs_t(L0_ffn_W2),
        "cols_in": np.concatenate([column(L0_xattn_bi), column(L0_xattn_bg), column(decay), column(L0_ffn_b1), gates],
                                  axis=1),
        "rows_in": np.broadcast_to(np.stack([np.asarray(L0_xattn_bo), np.asarray(L0_ffn_b2)])[None], (P, 2, D)),
    }
    nc = bacc.Bacc("TRN2", target_bir_lowering=False, num_devices=1)
    arrays = {n: np.ascontiguousarray(a) for n, a in arrays.items()}
    args = [nc.dram_tensor(n, a.shape, mybir.dt.from_np(a.dtype), kind="ExternalInput").ap() for n, a in arrays.items()]
    args.append(nc.dram_tensor("y_out", (NC, P, TILES, D), mybir.dt.float32, kind="ExternalOutput").ap())
    build(nc, *args)
    result = run_bass_kernel_spmd(nc, [arrays], core_ids=[0]).results[0]["y_out"]
    return np.ascontiguousarray(result.reshape(NC, STEPS, B, TILES, D).transpose(2, 0, 3, 1, 4).reshape(B, S, D))
```
